# Optimizing a Trainium2 kernel written in Bass

```python
import numpy as np
import jax
import jax.numpy as jnp

def _softmax(x, axis=-1):
    return jax.nn.softmax(x, axis=axis)

def _gelu(x):
    return jax.nn.gelu(x, approximate=True)

def _silu(x):
    return jax.nn.silu(x)

def _sigmoid(x):
    return jax.nn.sigmoid(x)

def _layernorm(x, axis=-1, eps=1e-05):
    m = jnp.mean(x, axis=axis, keepdims=True)
    v = jnp.var(x, axis=axis, keepdims=True)
    return (x - m) / jnp.sqrt(v + eps)

def _scatter_add(tgt, idx, src, axis=0):
    return tgt.at[idx].add(src)

def _segment_sum(src, seg, n):
    return jax.ops.segment_sum(src, seg, n)
kernel_name = 'mk_dlrm_tower_d1_rec_r8_e1c05f'

def setup_inputs(seed: int=0):
    np.random.seed(seed)
    _w = jnp.asarray

    def _rec_inputs():
        import jax
        import jax.numpy as jnp
        _tk = jax.random.key(seed)
        dense_ctx = jax.random.normal(jax.random.fold_in(_tk, 190), (2048, 16), jnp.float32)
        ids = jnp.stack([jax.random.randint(jax.random.fold_in(_tk, 200 + f), (2048,), 0, v, jnp.int32) for f, v in enumerate([12500, 1000, 1250, 1000, 12500, 12500, 1250, 1250, 12500, 1250, 125000, 125000, 1000, 12500, 1250, 12500, 12500, 12500, 1000, 12500, 1250, 12500, 1250, 1000, 1000, 12500, 12500, 12500, 1000, 1250, 1000, 1250, 1000, 12500, 1250, 1000, 12500, 1250, 1250, 1250])], axis=1)
        tbl_0 = 0.05 * jax.random.normal(jax.random.fold_in(_tk, 500 + 0), (12500, 64), jnp.float32)
        tbl_1 = 0.05 * jax.random.normal(jax.random.fold_in(_tk, 500 + 1), (1000, 64), jnp.float32)
        tbl_2 = 0.05 * jax.random.normal(jax.random.fold_in(_tk, 500 + 2), (1250, 64), jnp.float32)
        tbl_3 = 0.05 * jax.random.normal(jax.random.fold_in(_tk, 500 + 3), (1000, 64), jnp.float32)
        tbl_4 = 0.05 * jax.random.normal(jax.random.fold_in(_tk, 500 + 4), (12500, 64), jnp.float32)
        tbl_5 = 0.05 * jax.random.normal(jax.random.fold_in(_tk, 500 + 5), (12500, 64), jnp.float32)
        tbl_6 = 0.05 * jax.random.normal(jax.random.fold_in(_tk, 500 + 6), (1250, 64), jnp.float32)
        tbl_7 = 0.05 * jax.random.normal(jax.random.fold_in(_tk, 500 + 7), (1250, 64), jnp.float32)
        tbl_8 = 0.05 * jax.random.normal(jax.random.fold_in(_tk, 500 + 8), (12500, 64), jnp.float32)
        tbl_9 = 0.05 * jax.random.normal(jax.random.fold_in(_tk, 500 + 9), (1250, 64), jnp.float32)
        tbl_10 = 0.05 * jax.random.normal(jax.random.fold_in(_tk, 500 + 10), (125000, 64), jnp.float32)
        tbl_11 = 0.05 * jax.random.normal(jax.random.fold_in(_tk, 500 + 11), (125000, 64), jnp.float32)
        tbl_12 = 0.05 * jax.random.normal(jax.random.fold_in(_tk, 500 + 12), (1000, 64), jnp.float32)
        tbl_13 = 0.05 * jax.random.normal(jax.random.fold_in(_tk, 500 + 13), (12500, 64), jnp.float32)
        tbl_14 = 0.05 * jax.random.normal(jax.random.fold_in(_tk, 500 + 14), (1250, 64), jnp.float32)
        tbl_15 = 0.05 * jax.random.normal(jax.random.fold_in(_tk, 500 + 15), (12500, 64), jnp.float32)
        tbl_16 = 0.05 * jax.random.normal(jax.random.fold_in(_tk, 500 + 16), (12500, 64), jnp.float32)
        tbl_17 = 0.05 * jax.random.normal(jax.random.fold_in(_tk, 500 + 17), (12500, 64), jnp.float32)
        tbl_18 = 0.05 * jax.random.normal(jax.random.fold_in(_tk, 500 + 18), (1000, 64), jnp.float32)
        tbl_19 = 0.05 * jax.random.normal(jax.random.fold_in(_tk, 500 + 19), (12500, 64), jnp.float32)
        tbl_20 = 0.05 * jax.random.normal(jax.random.fold_in(_tk, 500 + 20), (1250, 64), jnp.float32)
        tbl_21 = 0.05 * jax.random.normal(jax.random.fold_in(_tk, 500 + 21), (12500, 64), jnp.float32)
        tbl_22 = 0.05 * jax.random.normal(jax.random.fold_in(_tk, 500 + 22), (1250, 64), jnp.float32)
        tbl_23 = 0.05 * jax.random.normal(jax.random.fold_in(_tk, 500 + 23), (1000, 64), jnp.float32)
        tbl_24 = 0.05 * jax.random.normal(jax.random.fold_in(_tk, 500 + 24), (1000, 64), jnp.float32)
        tbl_25 = 0.05 * jax.random.normal(jax.random.fold_in(_tk, 500 + 25), (12500, 64), jnp.float32)
        tbl_26 = 0.05 * jax.random.normal(jax.random.fold_in(_tk, 500 + 26), (12500, 64), jnp.float32)
        tbl_27 = 0.05 * jax.random.normal(jax.random.fold_in(_tk, 500 + 27), (12500, 64), jnp.float32)
        tbl_28 = 0.05 * jax.random.normal(jax.random.fold_in(_tk, 500 + 28), (1000, 64), jnp.float32)
        tbl_29 = 0.05 * jax.random.normal(jax.random.fold_in(_tk, 500 + 29), (1250, 64), jnp.float32)
        tbl_30 = 0.05 * jax.random.normal(jax.random.fold_in(_tk, 500 + 30), (1000, 64), jnp.float32)
        tbl_31 = 0.05 * jax.random.normal(jax.random.fold_in(_tk, 500 + 31), (1250, 64), jnp.float32)
        tbl_32 = 0.05 * jax.random.normal(jax.random.fold_in(_tk, 500 + 32), (1000, 64), jnp.float32)
        tbl_33 = 0.05 * jax.random.normal(jax.random.fold_in(_tk, 500 + 33), (12500, 64), jnp.float32)
        tbl_34 = 0.05 * jax.random.normal(jax.random.fold_in(_tk, 500 + 34), (1250, 64), jnp.float32)
        tbl_35 = 0.05 * jax.random.normal(jax.random.fold_in(_tk, 500 + 35), (1000, 64), jnp.float32)
        tbl_36 = 0.05 * jax.random.normal(jax.random.fold_in(_tk, 500 + 36), (12500, 64), jnp.float32)
        tbl_37 = 0.05 * jax.random.normal(jax.random.fold_in(_tk, 500 + 37), (1250, 64), jnp.float32)
        tbl_38 = 0.05 * jax.random.normal(jax.random.fold_in(_tk, 500 + 38), (1250, 64), jnp.float32)
        tbl_39 = 0.05 * jax.random.normal(jax.random.fold_in(_tk, 500 + 39), (1250, 64), jnp.float32)
        _rk = jax.random.fold_in(_tk, 7)
        W_top1 = 0.0354441 * jax.random.normal(jax.random.fold_in(_tk, 801), (796, 512), jnp.float32)
        W_top2 = 0.0441942 * jax.random.normal(jax.random.fold_in(_tk, 802), (512, 256), jnp.float32)
        W_top3 = 0.0625 * jax.random.normal(jax.random.fold_in(_tk, 803), (256, 1), jnp.float32)
        b_top1 = jnp.zeros((512,), jnp.float32)
        b_top2 = jnp.zeros((256,), jnp.float32)
        return (dense_ctx, ids, tbl_0, tbl_1, tbl_2, tbl_3, tbl_4, tbl_5, tbl_6, tbl_7, tbl_8, tbl_9, tbl_10, tbl_11, tbl_12, tbl_13, tbl_14, tbl_15, tbl_16, tbl_17, tbl_18, tbl_19, tbl_20, tbl_21, tbl_22, tbl_23, tbl_24, tbl_25, tbl_26, tbl_27, tbl_28, tbl_29, tbl_30, tbl_31, tbl_32, tbl_33, tbl_34, tbl_35, tbl_36, tbl_37, tbl_38, tbl_39, W_top1, b_top1, W_top2, b_top2, W_top3)
    dense_ctx, ids, tbl_0, tbl_1, tbl_2, tbl_3, tbl_4, tbl_5, tbl_6, tbl_7, tbl_8, tbl_9, tbl_10, tbl_11, tbl_12, tbl_13, tbl_14, tbl_15, tbl_16, tbl_17, tbl_18, tbl_19, tbl_20, tbl_21, tbl_22, tbl_23, tbl_24, tbl_25, tbl_26, tbl_27, tbl_28, tbl_29, tbl_30, tbl_31, tbl_32, tbl_33, tbl_34, tbl_35, tbl_36, tbl_37, tbl_38, tbl_39, W_top1, b_top1, W_top2, b_top2, W_top3 = _rec_inputs()

    def _L0_rec_setup():
        import jax, jax.numpy as jnp
        import numpy as np
        B, N, E = (1024, 40, 64)
        P = N * (N - 1) // 2

        def _pair_indices(n):
            row, col = ([], [])
            for i in range(n - 1):
                for j in range(i + 1, n):
                    row.append(i)
                    col.append(j)
            return (np.asarray(row), np.asarray(col))
        key = jax.random.key(seed)
        k1, k2 = jax.random.split(key)
        inputs = jax.random.normal(k1, (B, N, E), dtype=jnp.float32)
        std = float(np.sqrt(2.0 / (E + E)))
        param = jax.random.normal(k2, (E, P, E), dtype=jnp.float32) * std
        return {'inputs': inputs, 'param': param}
    _L0_rec_all = _L0_rec_setup()
    _L0_rec_in = {k: v for k, v in _L0_rec_all.items() if k in ('param',)}
    del _L0_rec_all
    return {'dense_ctx': dense_ctx, 'ids': ids, 'tbl_0': tbl_0, 'tbl_1': tbl_1, 'tbl_2': tbl_2, 'tbl_3': tbl_3, 'tbl_4': tbl_4, 'tbl_5': tbl_5, 'tbl_6': tbl_6, 'tbl_7': tbl_7, 'tbl_8': tbl_8, 'tbl_9': tbl_9, 'tbl_10': tbl_10, 'tbl_11': tbl_11, 'tbl_12': tbl_12, 'tbl_13': tbl_13, 'tbl_14': tbl_14, 'tbl_15': tbl_15, 'tbl_16': tbl_16, 'tbl_17': tbl_17, 'tbl_18': tbl_18, 'tbl_19': tbl_19, 'tbl_20': tbl_20, 'tbl_21': tbl_21, 'tbl_22': tbl_22, 'tbl_23': tbl_23, 'tbl_24': tbl_24, 'tbl_25': tbl_25, 'tbl_26': tbl_26, 'tbl_27': tbl_27, 'tbl_28': tbl_28, 'tbl_29': tbl_29, 'tbl_30': tbl_30, 'tbl_31': tbl_31, 'tbl_32': tbl_32, 'tbl_33': tbl_33, 'tbl_34': tbl_34, 'tbl_35': tbl_35, 'tbl_36': tbl_36, 'tbl_37': tbl_37, 'tbl_38': tbl_38, 'tbl_39': tbl_39, 'W_top1': W_top1, 'b_top1': b_top1, 'W_top2': W_top2, 'b_top2': b_top2, 'W_top3': W_top3, 'L0_rec_param': _L0_rec_in['param']}

def reference(dense_ctx, ids, tbl_0, tbl_1, tbl_2, tbl_3, tbl_4, tbl_5, tbl_6, tbl_7, tbl_8, tbl_9, tbl_10, tbl_11, tbl_12, tbl_13, tbl_14, tbl_15, tbl_16, tbl_17, tbl_18, tbl_19, tbl_20, tbl_21, tbl_22, tbl_23, tbl_24, tbl_25, tbl_26, tbl_27, tbl_28, tbl_29, tbl_30, tbl_31, tbl_32, tbl_33, tbl_34, tbl_35, tbl_36, tbl_37, tbl_38, tbl_39, W_top1, b_top1, W_top2, b_top2, W_top3, L0_rec_param):
    import jax
    import jax.numpy as jnp

    def _L0_rec_ref(inputs, param):
        import jax, jax.numpy as jnp
        import numpy as np
        B, N, E = (1024, 40, 64)
        P = N * (N - 1) // 2

        def _pair_indices(n):
            row, col = ([], [])
            for i in range(n - 1):
                for j in range(i + 1, n):
                    row.append(i)
                    col.append(j)
            return (np.asarray(row), np.asarray(col))
        n = inputs.shape[1]
        rowidx, colidx = _pair_indices(n)
        p = inputs[:, rowidx]
        q = inputs[:, colidx]
        out = jnp.einsum('bie,fie,bif->bi', p, param, q)
        return out[:, None, :]
    e = jnp.stack([tbl_0[ids[:, 0]], tbl_1[ids[:, 1]], tbl_2[ids[:, 2]], tbl_3[ids[:, 3]], tbl_4[ids[:, 4]], tbl_5[ids[:, 5]], tbl_6[ids[:, 6]], tbl_7[ids[:, 7]], tbl_8[ids[:, 8]], tbl_9[ids[:, 9]], tbl_10[ids[:, 10]], tbl_11[ids[:, 11]], tbl_12[ids[:, 12]], tbl_13[ids[:, 13]], tbl_14[ids[:, 14]], tbl_15[ids[:, 15]], tbl_16[ids[:, 16]], tbl_17[ids[:, 17]], tbl_18[ids[:, 18]], tbl_19[ids[:, 19]], tbl_20[ids[:, 20]], tbl_21[ids[:, 21]], tbl_22[ids[:, 22]], tbl_23[ids[:, 23]], tbl_24[ids[:, 24]], tbl_25[ids[:, 25]], tbl_26[ids[:, 26]], tbl_27[ids[:, 27]], tbl_28[ids[:, 28]], tbl_29[ids[:, 29]], tbl_30[ids[:, 30]], tbl_31[ids[:, 31]], tbl_32[ids[:, 32]], tbl_33[ids[:, 33]], tbl_34[ids[:, 34]], tbl_35[ids[:, 35]], tbl_36[ids[:, 36]], tbl_37[ids[:, 37]], tbl_38[ids[:, 38]], tbl_39[ids[:, 39]]], axis=1)
    z = _L0_rec_ref(e, L0_rec_param)
    z = z.reshape(z.shape[0], -1)
    h = jnp.concatenate([z, dense_ctx], axis=1)
    h = jnp.maximum(h @ W_top1 + b_top1, 0.0)
    h = jnp.maximum(h @ W_top2 + b_top2, 0.0)
    y = h @ W_top3
    return y

_drawn_inputs = setup_inputs


def setup_inputs(seed=0):
    import zlib

    import numpy as np

    out = dict(_drawn_inputs(seed))
    spreads = {'b_top1': (0.0, 0.1), 'b_top2': (0.0, 0.1)}
    factors = {}
    for name, (base, spread) in spreads.items():
        noise = np.random.default_rng([zlib.crc32(name.encode()), seed]).standard_normal(out[name].shape)
        drawn = base * np.exp(spread * noise) if base else spread * noise
        out[name] = jnp.asarray(drawn.astype(out[name].dtype))
    for name, factor in factors.items():
        out[name] = (out[name] * factor).astype(out[name].dtype)
    return out
```

```python
import numpy as np

import concourse.bass as bass
import concourse.mybir as mybir

FIELDS, E, BATCH, DENSE = 40, 64, 2048, 16
H1, H2 = 512, 256
P = 128
B = 512
CHUNKS = BATCH // B
ROWT = B // P
KP = FIELDS // 2
TILES = [(k, i) for k in range(KP) for i in range(2 * k + 1)]
NT = len(TILES)
NP = NT // 2
WT = 4
NW = NT // WT
ZT = 64
NZ = -(-NT // ZT)
LAST_ROWS_FREE = 8

G_SLOTS, Q_SLOTS, W_SLOTS, T_SLOTS, R_SLOTS = 10, 4, 5, 2, 3
W_ON_VECTOR = (1, 3)
W_ON_POOL = tuple(s for s in range(W_SLOTS) if s not in W_ON_VECTOR)
RED_LAG = 2


def pair_index(i, j):
    return i * FIELDS - i * (i + 1) // 2 + j - i - 1


def z_row(t, half):
    block, u = divmod(t, ZT)
    return block * P + 32 * (u % 4) + 2 * (u // 4) + half


def prep_at(k):
    return max(0, (k * k - 12) // 2)


def build(nc, dense_t, ids, tables, w_tiles, w1, b1, w2, b2, w3, y):
    from contextlib import ExitStack

    f32, f32r, i32 = mybir.dt.float32, mybir.dt.float32r, mybir.dt.int32
    ALU, ACT = mybir.AluOpType, mybir.ActivationFunctionType

    with ExitStack() as ctx:
        def sb(name, shape, dt=f32):
            return ctx.enter_context(nc.sbuf_tensor(name, shape, dt))

        def sem(name):
            return ctx.enter_context(nc.semaphore(name))

        ids_all = sb("ids_all", [P, BATCH // P, FIELDS], i32)
        ids_early = sb("ids_early", [P, ROWT, FIELDS // 2], i32)
        ids_late = sb("ids_late", [P, ROWT, FIELDS // 2], i32)
        rows = sb("rows", [P, G_SLOTS, ROWT, 2 * E])
        ident = sb("ident", [P, 8 + P])
        ones = sb("ones", [P, 62])
        q = sb("q", [P, Q_SLOTS, B])
        p = sb("p", [P, FIELDS - 1, B], f32r)
        w_raw = sb("w_raw", [P, W_SLOTS, WT * P])
        w_hi = sb("w_hi", [P, W_SLOTS, WT * P], f32r)
        w_lo = sb("w_lo", [P, W_SLOTS, WT * P], f32r)
        product = sb("product", [P, R_SLOTS, 2, B])
        z = sb("z", [P, NZ, B])
        dense_sb = sb("dense_sb", [DENSE, B])
        w1_sb = sb("w1_sb", [P, NZ, H1])
        w2_sb = sb("w2_sb", [P, H1 // P, H2])
        w3_sb = sb("w3_sb", [P, H2 // P])
        b1_sb = sb("b1_sb", [P, H1 // P])
        b2_sb = sb("b2_sb", [P, H2 // P])
        h1 = sb("h1", [P, H1 // P, B])
        h2 = sb("h2", [P, H2 // P, B])
        y_sb = sb("y_sb", [1, BATCH])
        t_ps = ctx.enter_context(nc.psum_tensor("t_ps", [P, T_SLOTS, 2, B], f32))
        z_ps = ctx.enter_context(nc.psum_tensor("z_ps", [P, 2, B], f32))
        x_ps = ctx.enter_context(nc.psum_tensor("x_ps", [P, 2, B], f32))

        ids_in = sem("ids_in")
        layers_in = sem("layers_in")
        dense_in = sem("dense_in")
        y_out = sem("y_out")
        ident_ready = sem("ident_ready")
        ones_ready = sem("ones_ready")
        ids_ready = sem("ids_ready")
        lookups_begun = sem("lookups_begun")
        raw_in = [sem(f"raw_in{s}") for s in range(W_SLOTS)]
        rows_in = [sem(f"rows_in{s}") for s in range(G_SLOTS)]
        x_ready = sem("x_ready")
        lo_vector = sem("lo_vector")
        lo_pool = sem("lo_pool")
        FREE_X, FREE_V, FREE_P, FREE_L = G_SLOTS, len(W_ON_VECTOR), len(W_ON_POOL), 2
        e_hi = sem("e_hi")
        e_ready = sem("e_ready")
        hi_ready = sem("hi_ready")
        t_ready = sem("t_ready")
        product_ready = sem("product_ready")
        summed = sem("summed")
        z_ready = sem("z_ready")
        layer_ps = sem("layer_ps")
        layer_sb = sem("layer_sb")
        PIECES = H1 // P + H2 // P + 1

        block = ctx.enter_context(nc.Block())

        def lo_of(g):
            turn, s = divmod(g, W_SLOTS)
            if s in W_ON_VECTOR:
                return lo_vector, len(W_ON_VECTOR) * KW, len(W_ON_VECTOR) * turn + W_ON_VECTOR.index(s), FREE_V
            return lo_pool, len(W_ON_POOL) * KW, len(W_ON_POOL) * turn + W_ON_POOL.index(s), FREE_P

        KW = NW // W_SLOTS

        @block.sync
        def _(sp):
            sp.dma_start(ids_all[:], ids.rearrange("(t p) f -> p t f", p=P)).then_inc(ids_in, 16)

            def load_granules(c, j):
                for s in range(W_SLOTS):
                    free, _, n, _ = lo_of(s)
                    per_turn = len(W_ON_VECTOR) if s in W_ON_VECTOR else len(W_ON_POOL)
                    sp.wait_ge(free, c * (per_turn * KW) + j * per_turn + (n + 1))
                    col = j * (W_SLOTS * WT * P) + s * WT * P
                    for half in range(2):
                        sp.dma_start(w_raw[64 * half:64 * half + 64, s, :], w_tiles[:, bass.ds(col, WT * P)])\
                          .then_inc(raw_in[s], 16)

            load_granules(0, 0)
            sp.dma_start(w1_sb[:], w1).then_inc(layers_in, 16)
            sp.dma_start(b1_sb[:], b1).then_inc(layers_in, 16)
            sp.dma_start(w2_sb[:], w2).then_inc(layers_in, 16)
            sp.dma_start(b2_sb[:], b2).then_inc(layers_in, 16)
            sp.dma_start(w3_sb[:], w3).then_inc(layers_in, 16)
            with sp.Fori(1, KW) as j:
                load_granules(0, j)
            with sp.Fori(1, CHUNKS) as c:
                with sp.Fori(0, KW) as j:
                    load_granules(c, j)

        @block.gpsimd
        def _(pool):
            def copy_ids(c, late, nth):
                dst = ids_late if late else ids_early
                src = ids_all[:, bass.ds(c * ROWT, ROWT), (FIELDS // 2) * late:(FIELDS // 2) * (late + 1)]
                nc.gpsimd.tensor_copy(dst[:], src).then_inc(ids_ready, 1)
                pool.wait_ge(ids_ready, nth)
                pool.sem_inc(lookups_begun, 1)

            def lookup(c, k, m):
                t, h = divmod(m, 2)
                if m == 0:
                    pool.wait_ge(x_ready, c * KP + (k + 1))
                    pool.sem_inc(lookups_begun, 1)
                late, col = divmod(2 * k + h, FIELDS // 2)
                idx = (ids_late if late else ids_early)[:, t, col:col + 1]
                nc.gpsimd.indirect_dma_start(
                    rows[:, k % G_SLOTS, t, h * E:(h + 1) * E], None, tables[2 * k + h],
                    bass.IndirectOffsetOnAxis(idx, axis=0)).then_inc(rows_in[k % G_SLOTS], 16)

            def low_weights(c, g):
                s = g % W_SLOTS
                pool.wait_ge(hi_ready, c * NW + (g + 1))
                nc.gpsimd.tensor_tensor(w_lo[:, s, :], w_raw[:, s, :], w_hi[:, s, :].bitcast(f32),
                                        ALU.subtract).then_inc(lo_pool, 1)

            def chunk(c, first, last):
                for n in range(NP):
                    if n == 0 and not first:
                        copy_ids(c, 1, c * 2 + 2)
                    if n == NP // 2 and not last:
                        copy_ids(c + 1, 0, c * 2 + 3)
                    for k in range(KP):
                        for m in range(2 * ROWT):
                            if k >= KP // 2 or first:
                                at = (k - KP // 2) * 10 + m if not first else min(max(0, (k * k - 12) // 2 - 12), 9 * k)
                                if at == n:
                                    lookup(c, k, m)
                            if k < KP // 2 and not last and NP // 2 + 10 * k + m == n:
                                lookup(c + 1, k, m)
                    for g in range(NW):
                        if g % W_SLOTS in W_ON_POOL and max(0, 2 * g - 5) == n:
                            low_weights(c, g)

            pool.wait_ge(ids_in, 16)
            copy_ids(0, 0, 1)
            copy_ids(0, 1, 2)
            pool.sem_inc(lo_pool, FREE_P)
            nc.gpsimd.memset(ident[:], 0.0).then_inc(ident_ready, 1)
            pool.wait_ge(ident_ready, 1)
            nc.gpsimd.affine_select(out=ident[:], in_=ident[:], compare_op=ALU.not_equal, fill=1.0, base=8,
                                    pattern=[[-1, 8 + P]], channel_multiplier=1).then_inc(ident_ready, 1)
            pool.wait_ge(ident_ready, 2)
            chunk(0, True, False)
            with pool.Fori(1, CHUNKS - 1) as c:
                chunk(c, False, False)
            chunk(CHUNKS - 1, False, True)

        @block.scalar
        def _(act):
            def high_parts(c, k):
                act.wait_ge(x_ready, c * KP + (FREE_X + k + 1))
                if k >= Q_SLOTS:
                    act.wait_ge(product_ready, c * NP + (k - Q_SLOTS + 1) ** 2 // 2 + 1)
                x = x_ps[:, k % 2, :]
                nc.scalar.copy(q[:, k % Q_SLOTS, :], x)
                last = nc.scalar.copy(p[0:64, 2 * k, :], x[0:64, :])
                if 2 * k + 1 < FIELDS - 1:
                    last = nc.scalar.copy(p[64:128, 2 * k + 1, :], x[64:128, :])
                last.then_inc(e_hi, 1)

            def high_weights(c, g):
                s = g % W_SLOTS
                if g >= W_SLOTS:
                    act.wait_ge(t_ready, c * NP + 2 * (g - W_SLOTS) + 2)
                act.wait_ge(raw_in[s], c * (32 * KW) + 32 * (g // W_SLOTS + 1))
                nc.scalar.copy(w_hi[:, s, :], w_raw[:, s, :]).then_inc(hi_ready, 1)

            def keep_z(c, block_):
                act.wait_ge(summed, c * NP + min((block_ + 1) * ZT // 2, NP))
                nc.scalar.copy(z[:, block_, :], z_ps[:, block_ % 2, :]).then_inc(z_ready, 1)

            act.sem_inc(layer_sb, FREE_L)
            with act.Fori(0, CHUNKS) as c:
                act.dma_start(dense_sb[:], dense_t[:, bass.ds(c * B, B)]).then_inc(dense_in, 16)
                for n in range(NP):
                    for k in range(KP):
                        if prep_at(k) == n:
                            high_parts(c, k)
                    for g in range(NW):
                        if max(0, 2 * g - 6) == n:
                            high_weights(c, g)
                    for blk in range(NZ - 1):
                        if (blk + 1) * ZT // 2 + RED_LAG + 1 == n:
                            keep_z(c, blk)
                keep_z(c, NZ - 1)
                act.wait_ge(layers_in, 80)
                for m in range(H1 // P):
                    act.wait_ge(layer_ps, c * PIECES + (m + 1))
                    nc.scalar.activation(h1[:, m, :], x_ps[:, m % 2, :], ACT.Relu, bias=b1_sb[:, m:m + 1])\
                      .then_inc(layer_sb, 1)
                for m in range(H2 // P):
                    act.wait_ge(layer_ps, c * PIECES + (H1 // P + m + 1))
                    nc.scalar.activation(h2[:, m, :], x_ps[:, m % 2, :], ACT.Relu, bias=b2_sb[:, m:m + 1])\
                      .then_inc(layer_sb, 1)
                act.wait_ge(layer_ps, c * PIECES + PIECES)
                nc.scalar.copy(y_sb[:, bass.ds(c * B, B)], x_ps[0:1, 0, :]).then_inc(layer_sb, 1)
            act.wait_ge(layer_sb, CHUNKS * PIECES + FREE_L)
            act.dma_start(y, y_sb[:]).then_inc(y_out, 16)
            act.wait_ge(y_out, 16)

        @block.vector
        def _(dve):
            def low_parts(c, k):
                dve.wait_ge(e_hi, c * KP + (k + 1))
                x = x_ps[:, k % 2, :]
                last = nc.vector.tensor_tensor(p[64:128, 2 * k, :], x[0:64, :], p[0:64, 2 * k, :].bitcast(f32),
                                               ALU.subtract)
                if 2 * k + 1 < FIELDS - 1:
                    last = nc.vector.tensor_tensor(p[0:64, 2 * k + 1, :], x[64:128, :],
                                                   p[64:128, 2 * k + 1, :].bitcast(f32), ALU.subtract)
                last.then_inc(e_ready, 1)

            def low_weights(c, g):
                s = g % W_SLOTS
                dve.wait_ge(hi_ready, c * NW + (g + 1))
                nc.vector.tensor_tensor(w_lo[:, s, :], w_raw[:, s, :], w_hi[:, s, :].bitcast(f32),
                                        ALU.subtract).then_inc(lo_vector, 1)

            def products(c, n):
                k0, k1 = TILES[2 * n][0], TILES[2 * n + 1][0]
                if n >= R_SLOTS:
                    dve.wait_ge(summed, c * NP + (n - R_SLOTS + 1))
                dve.wait_ge(t_ready, c * NP + (n + 1))
                out, t = product[:, n % R_SLOTS, :, :], t_ps[:, n % T_SLOTS, :, :]
                if k0 == k1:
                    both = q[:, k0 % Q_SLOTS:k0 % Q_SLOTS + 1, :].to_broadcast([P, 2, B])
                    nc.vector.tensor_tensor(out, t, both, ALU.mult).then_inc(product_ready, 1)
                else:
                    nc.vector.tensor_tensor(out[:, 0, :], t[:, 0, :], q[:, k0 % Q_SLOTS, :], ALU.mult)
                    nc.vector.tensor_tensor(out[:, 1, :], t[:, 1, :], q[:, k1 % Q_SLOTS, :], ALU.mult)\
                      .then_inc(product_ready, 1)

            dve.sem_inc(lo_vector, FREE_V)
            nc.vector.memset(ones[:], 0.0).then_inc(ones_ready, 1)
            dve.wait_ge(ones_ready, 1)
            nc.vector.memset(ones[0:64, 30:31], 1.0).then_inc(ones_ready, 1)
            nc.vector.memset(ones[64:128, 31:32], 1.0).then_inc(ones_ready, 1)
            with dve.Fori(0, CHUNKS) as c:
                for n in range(NP):
                    for k in range(KP):
                        if prep_at(k) == n:
                            low_parts(c, k)
                    for g in range(NW):
                        if g % W_SLOTS in W_ON_VECTOR and max(0, 2 * g - 5) == n:
                            low_weights(c, g)
                    products(c, n)

        @block.tensor
        def _(pe):
            def transpose_rows(c, k):
                if k >= 2:
                    pe.wait_ge(e_ready, c * KP + (k - 1))
                pe.wait_ge(rows_in[k % G_SLOTS],
                           c * (KP // G_SLOTS * 128) + 128 * (k // G_SLOTS + 1))
                for t in range(ROWT):
                    last = nc.tensor.transpose(x_ps[:, k % 2, t * P:(t + 1) * P],
                                               rows[:, k % G_SLOTS, t, :], ident[:, 8:8 + P])
                last.then_inc(x_ready, 1)

            def multiply(c, n):
                g = 2 * n // WT
                if 2 * n % WT == 0:
                    done, per_chunk, nth, start = lo_of(g)
                    pe.wait_ge(done, c * per_chunk + (start + nth + 1))
                if n >= T_SLOTS:
                    pe.wait_ge(product_ready, c * NP + (n - T_SLOTS + 1))
                for h in range(2):
                    k, i = TILES[2 * n + h]
                    if i == 0:
                        pe.wait_ge(e_ready, c * KP + (k + 1))
                    w = slice((2 * n + h) % WT * P, ((2 * n + h) % WT + 1) * P)
                    nc.tensor.matmul(t_ps[:, n % T_SLOTS, h, :], w_lo[:, g % W_SLOTS, w], p[:, i, :],
                                     start=True, stop=False)
                    last = nc.tensor.matmul(t_ps[:, n % T_SLOTS, h, :], w_hi[:, g % W_SLOTS, w], p[:, i, :],
                                            start=False, stop=True)
                last.then_inc(t_ready, 1)

            def sum_features(c, n):
                if 2 * n == (NZ - 1) * ZT:
                    pe.wait_ge(dense_in, c * 16 + 16)
                pe.wait_ge(product_ready, c * NP + (n + 1))
                for h in range(2):
                    blk, u = divmod(2 * n + h, ZT)
                    group, s = u % 4, u // 4
                    if u == 0 and blk >= 2:
                        pe.wait_ge(z_ready, c * NZ + (blk - 1))
                    last_of_group = min(ZT, NT - blk * ZT) // 4 - 1
                    last = nc.tensor.matmul(z_ps[32 * group:32 * group + 32, blk % 2, :],
                                            ones[:, 30 - 2 * s:62 - 2 * s], product[:, n % R_SLOTS, h, :],
                                            start=(s == 0), stop=(s == last_of_group))
                    if blk == NZ - 1 and u == 0:
                        nc.tensor.matmul(z_ps[0:32, blk % 2, :], ident[0:DENSE, 0:32], dense_sb[:, :],
                                         start=False, stop=False)
                last.then_inc(summed, 1)

            def layer(c, first_piece, pieces, weights, x, kt):
                for m in range(pieces):
                    piece = first_piece + m
                    if piece >= 2:
                        pe.wait_ge(layer_sb, c * PIECES + (FREE_L + piece - 1))
                    for j in range(kt):
                        last = nc.tensor.matmul(x_ps[:, piece % 2, :], weights[:, j, m * P:(m + 1) * P],
                                                x[:, j, :], start=(j == 0), stop=(j == kt - 1))
                    last.then_inc(layer_ps, 1)

            pe.sem_inc(x_ready, FREE_X)
            pe.wait_ge(ident_ready, 2)
            pe.wait_ge(ones_ready, 3)
            with pe.Fori(0, CHUNKS) as c:
                pe.wait_ge(layer_sb, c * PIECES + FREE_L)
                for n in range(NP):
                    for k in range(KP):
                        if prep_at(k) == n:
                            transpose_rows(c, k)
                    multiply(c, n)
                    if n >= RED_LAG:
                        sum_features(c, n - RED_LAG)
                for n in range(NP - RED_LAG, NP):
                    sum_features(c, n)
                pe.wait_ge(layers_in, 80)
                pe.wait_ge(z_ready, c * NZ + NZ)
                layer(c, 0, H1 // P, w1_sb, z, NZ)
                pe.wait_ge(layer_sb, c * PIECES + (FREE_L + H1 // P))
                layer(c, H1 // P, H2 // P, w2_sb, h1, H1 // P)
                pe.wait_ge(layer_sb, c * PIECES + (FREE_L + PIECES - 1))
                for j in range(H2 // P):
                    last = nc.tensor.matmul(x_ps[0:1, 0, :], w3_sb[:, j:j + 1], h2[:, j, :],
                                            start=(j == 0), stop=(j == H2 // P - 1))
                last.then_inc(layer_ps, 1)


def kernel(**inputs):
    import concourse.bacc as bacc
    from concourse.bass_utils import run_bass_kernel_spmd

    a = {n: np.asarray(v) for n, v in inputs.items()}

    param = a["L0_rec_param"]
    w_tiles = np.zeros((E, NT, 2, E), param.dtype)
    w1 = np.zeros((NZ * P, H1), a["W_top1"].dtype)
    for t, (k, i) in enumerate(TILES):
        for half in range(2):
            if i < 2 * k + half:
                w_tiles[:, t, half] = param[:, pair_index(i, 2 * k + half)].T
                w1[z_row(t, half)] = a["W_top1"][pair_index(i, 2 * k + half)]
    at = (NZ - 1) * P + LAST_ROWS_FREE
    w1[at:at + DENSE] = a["W_top1"][FIELDS * (FIELDS - 1) // 2:]

    def by_partition(x):
        return np.ascontiguousarray(x.reshape(-1, P, x.shape[-1]).transpose(1, 0, 2))

    arrays = {
        "dense_t": np.ascontiguousarray(a["dense_ctx"].T),
        "ids": np.ascontiguousarray(a["ids"]),
        "w_tiles": w_tiles.reshape(E, NT * P),
        "w1": by_partition(w1),
        "b1": np.ascontiguousarray(a["b_top1"].reshape(-1, P).T),
        "w2": by_partition(a["W_top2"]),
        "b2": np.ascontiguousarray(a["b_top2"].reshape(-1, P).T),
        "w3": np.ascontiguousarray(a["W_top3"].reshape(-1, P).T),
    }
    for f in range(FIELDS):
        arrays[f"tbl_{f}"] = np.ascontiguousarray(a[f"tbl_{f}"])

    nc = bacc.Bacc("TRN2", target_bir_lowering=False, num_devices=1)
    d = {n: nc.dram_tensor(n, v.shape, mybir.dt.from_np(v.dtype), kind="ExternalInput").ap()
         for n, v in arrays.items()}
    y = nc.dram_tensor("y", (1, BATCH), mybir.dt.float32, kind="ExternalOutput").ap()
    build(nc, d["dense_t"], d["ids"], [d[f"tbl_{f}"] for f in range(FIELDS)], d["w_tiles"],
          d["w1"], d["b1"], d["w2"], d["b2"], d["w3"], y)
    r = run_bass_kernel_spmd(nc, [arrays], core_ids=[0])
    return r.results[0]["y"].reshape(BATCH, 1)
```

```python
import numpy as np

import concourse.bass as bass
import concourse.mybir as mybir

FIELDS, E, BATCH, DENSE = 40, 64, 2048, 16
H1, H2 = 512, 256
P = 128
B = 512
CHUNKS = BATCH // B
ROWT = B // P
KP = FIELDS // 2
TILES = [(k, i) for k in range(KP) for i in range(2 * k + 1)]
NT = len(TILES)
NP = NT // 2
WT = 4
NW = NT // WT
ZT = 64
NZ = -(-NT // ZT)
LAST_ROWS_FREE = 8

G_SLOTS, Q_SLOTS, W_SLOTS, T_SLOTS, R_SLOTS = 10, 4, 5, 3, 6
W_ON_VECTOR = (1, 3)
W_ON_POOL = tuple(s for s in range(W_SLOTS) if s not in W_ON_VECTOR)
SUMS = 2
LAG = 2


def pair_index(i, j):
    return i * FIELDS - i * (i + 1) // 2 + j - i - 1


def z_row(t, half):
    block, u = divmod(t, ZT)
    return block * P + 32 * (u % 4) + 2 * (u // 4) + half


EARLY_K = 4
EARLY_W = 4


def prep_at(k):
    return (k * k - 12) // 2


def low_at(k):
    return min(prep_at(k) + 2, k * k // 2)


def build(nc, dense_t, ids, tables, w_tiles, w1, b1, w2, b2, w3, y):
    from contextlib import ExitStack

    f32, f32r, i32 = mybir.dt.float32, mybir.dt.float32r, mybir.dt.int32
    ALU, ACT = mybir.AluOpType, mybir.ActivationFunctionType

    with ExitStack() as ctx:
        def sb(name, shape, dt=f32):
            return ctx.enter_context(nc.sbuf_tensor(name, shape, dt))

        def sem(name):
            return ctx.enter_context(nc.semaphore(name))

        ids_all = sb("ids_all", [P, BATCH // P, FIELDS], i32)
        ids_early = sb("ids_early", [P, ROWT, FIELDS // 2], i32)
        ids_late = sb("ids_late", [P, ROWT, FIELDS // 2], i32)
        rows = sb("rows", [P, G_SLOTS, ROWT, 2 * E])
        ident = sb("ident", [P, 8 + P])
        ones = sb("ones", [P, 62])
        q = sb("q", [P, Q_SLOTS, B])
        p = sb("p", [P, FIELDS - 1, B], f32r)
        w_raw = sb("w_raw", [P, W_SLOTS, WT * P])
        w_hi = sb("w_hi", [P, W_SLOTS, WT * P], f32r)
        w_lo = sb("w_lo", [P, W_SLOTS, WT * P], f32r)
        product = sb("product", [P, R_SLOTS, 2, B])
        z = sb("z", [P, NZ, B])
        h1 = product[:, 0:H1 // P // 2, :, :].rearrange("p s h b -> p (s h) b")
        dense_sb = sb("dense_sb", [DENSE, B])
        w1_sb = sb("w1_sb", [P, NZ, H1])
        w2_sb = sb("w2_sb", [P, H1 // P, H2])
        w3_sb = sb("w3_sb", [P, H2 // P])
        b1_sb = sb("b1_sb", [P, H1 // P])
        b2_sb = sb("b2_sb", [P, H2 // P])
        h2 = z[:, 0:H2 // P, :]
        y_sb = sb("y_sb", [1, B])
        t_ps = ctx.enter_context(nc.psum_tensor("t_ps", [P, T_SLOTS, 2, B], f32))
        z_ps = ctx.enter_context(nc.psum_tensor("z_ps", [P, B], f32))
        x_ps = ctx.enter_context(nc.psum_tensor("x_ps", [P, B], f32))

        ids_in = sem("ids_in")
        layers_in = sem("layers_in")
        dense_in = sem("dense_in")
        y_out = sem("y_out")
        ident_ready = sem("ident_ready")
        ones_ready = sem("ones_ready")
        ids_ready = sem("ids_ready")
        lookups_begun = sem("lookups_begun")
        raw_in = [sem(f"raw_in{s}") for s in range(W_SLOTS)]
        rows_in = [sem(f"rows_in{s}") for s in range(G_SLOTS)]
        x_ready = sem("x_ready")
        lo_vector = sem("lo_vector")
        lo_pool = sem("lo_pool")
        FREE_X, FREE_V, FREE_P, FREE_L = G_SLOTS, len(W_ON_VECTOR), len(W_ON_POOL), 2
        e_hi = sem("e_hi")
        e_ready = sem("e_ready")
        hi_ready = sem("hi_ready")
        t_ready = sem("t_ready")
        product_ready = sem("product_ready")
        summed = sem("summed")
        z_ready = sem("z_ready")
        layer_ps = sem("layer_ps")
        layer_sb = sem("layer_sb")
        PIECES = H1 // P + H2 // P + 1

        block = ctx.enter_context(nc.Block())

        def lo_of(g):
            turn, s = divmod(g, W_SLOTS)
            if s in W_ON_VECTOR:
                return lo_vector, len(W_ON_VECTOR) * KW, len(W_ON_VECTOR) * turn + W_ON_VECTOR.index(s), FREE_V
            return lo_pool, len(W_ON_POOL) * KW, len(W_ON_POOL) * turn + W_ON_POOL.index(s), FREE_P

        def layer_bank(piece):
            return t_ps[:, piece // 2 % T_SLOTS, piece % 2, :]

        KW = NW // W_SLOTS

        @block.sync
        def _(sp):
            sp.dma_start(ids_all[:], ids.rearrange("(t p) f -> p t f", p=P)).then_inc(ids_in, 16)

            def load_granules(c, j):
                for s in range(W_SLOTS):
                    free, _, n, _ = lo_of(s)
                    per_turn = len(W_ON_VECTOR) if s in W_ON_VECTOR else len(W_ON_POOL)
                    sp.wait_ge(free, c * (per_turn * KW) + j * per_turn + (n + 1))
                    col = j * (W_SLOTS * WT * P) + s * WT * P
                    for half in range(2):
                        sp.dma_start(w_raw[64 * half:64 * half + 64, s, :], w_tiles[:, bass.ds(col, WT * P)])\
                          .then_inc(raw_in[s], 16)

            load_granules(0, 0)
            sp.dma_start(w1_sb[:], w1).then_inc(layers_in, 16)
            sp.dma_start(b1_sb[:], b1).then_inc(layers_in, 16)
            sp.dma_start(w2_sb[:], w2).then_inc(layers_in, 16)
            sp.dma_start(b2_sb[:], b2).then_inc(layers_in, 16)
            sp.dma_start(w3_sb[:], w3).then_inc(layers_in, 16)
            with sp.Fori(1, KW) as j:
                load_granules(0, j)
            with sp.Fori(1, CHUNKS) as c:
                with sp.Fori(0, KW) as j:
                    load_granules(c, j)

        @block.gpsimd
        def _(pool):
            def copy_ids(c, late, nth):
                dst = ids_late if late else ids_early
                src = ids_all[:, bass.ds(c * ROWT, ROWT), (FIELDS // 2) * late:(FIELDS // 2) * (late + 1)]
                nc.gpsimd.tensor_copy(dst[:], src).then_inc(ids_ready, 1)
                pool.wait_ge(ids_ready, nth)
                pool.sem_inc(lookups_begun, 1)

            def lookup(c, k, m):
                t, h = divmod(m, 2)
                if m == 0:
                    pool.wait_ge(x_ready, c * KP + (k + 1))
                    pool.sem_inc(lookups_begun, 1)
                late, col = divmod(2 * k + h, FIELDS // 2)
                idx = (ids_late if late else ids_early)[:, t, col:col + 1]
                nc.gpsimd.indirect_dma_start(
                    rows[:, k % G_SLOTS, t, h * E:(h + 1) * E], None, tables[2 * k + h],
                    bass.IndirectOffsetOnAxis(idx, axis=0)).then_inc(rows_in[k % G_SLOTS], 16)

            def low_weights(c, g):
                s = g % W_SLOTS
                pool.wait_ge(hi_ready, c * NW + (g + 1))
                nc.gpsimd.tensor_tensor(w_lo[:, s, :], w_raw[:, s, :], w_hi[:, s, :].bitcast(f32),
                                        ALU.subtract).then_inc(lo_pool, 1)

            def lookup_at(k, m, first):
                if first:
                    return 0 if k < 4 else max(k * k // 2 - 12, 4 * k - 15) if k < 9 else 7 * k - 36 + m
                return (k - KP // 2) * 10 + m if k >= KP // 2 else -1

            def chunk(c, first, last):
                for n in range(NP):
                    if n == 0 and not first:
                        copy_ids(c, 1, c * 2 + 2)
                    if n == NP // 2 and not last:
                        copy_ids(c + 1, 0, c * 2 + 3)
                    for k in range(KP):
                        for m in range(2 * ROWT):
                            if lookup_at(k, m, first) == n:
                                lookup(c, k, m)
                            if k < KP // 2 and not last and NP // 2 + (8 if first else 10) * k + m == n:
                                lookup(c + 1, k, m)
                        if first and n == 0 and k < 2:
                            for g in FIRST_LOWS[k]:
                                low_weights(c, g)
                    for g in range(NW):
                        if g % W_SLOTS in W_ON_POOL and max(0, 2 * g - 5) == n and not (first and g < 3):
                            low_weights(c, g)

            FIRST_LOWS = [[g for g in gs if g in W_ON_POOL] for gs in ((0,), (1, 2))]
            pool.wait_ge(ids_in, 16)
            copy_ids(0, 0, 1)
            copy_ids(0, 1, 2)
            pool.sem_inc(lo_pool, FREE_P)
            nc.gpsimd.memset(ident[:], 0.0).then_inc(ident_ready, 1)
            pool.wait_ge(ident_ready, 1)
            nc.gpsimd.affine_select(out=ident[:], in_=ident[:], compare_op=ALU.not_equal, fill=1.0, base=8,
                                    pattern=[[-1, 8 + P]], channel_multiplier=1).then_inc(ident_ready, 1)
            pool.wait_ge(ident_ready, 2)
            chunk(0, True, False)
            with pool.Fori(1, CHUNKS - 1) as c:
                chunk(c, False, False)
            chunk(CHUNKS - 1, False, True)

        @block.scalar
        def _(act):
            def high_parts(c, k):
                act.wait_ge(x_ready, c * KP + (FREE_X + k + 1))
                if k >= Q_SLOTS:
                    act.wait_ge(product_ready, c * NP + (k - Q_SLOTS + 1) ** 2 // 2 + 1)
                x = x_ps[:, :]
                nc.scalar.copy(p[0:64, 2 * k, :], x[0:64, :])
                if 2 * k + 1 < FIELDS - 1:
                    nc.scalar.copy(p[64:128, 2 * k + 1, :], x[64:128, :])
                nc.scalar.copy(q[:, k % Q_SLOTS, :], x).then_inc(e_hi, 1)

            def high_weights(c, g):
                s = g % W_SLOTS
                if g >= W_SLOTS:
                    act.wait_ge(t_ready, c * NP + 2 * (g - W_SLOTS) + 2)
                act.wait_ge(raw_in[s], c * (32 * KW) + 32 * (g // W_SLOTS + 1))
                nc.scalar.copy(w_hi[:, s, :], w_raw[:, s, :]).then_inc(hi_ready, 1)

            def keep_z(c, block_):
                act.wait_ge(summed, c * NP + min((block_ + 1) * ZT // 2, NP))
                nc.scalar.copy(z[:, block_, :], z_ps[:, :]).then_inc(z_ready, 1)

            def chunk(c, first, last):
                act.dma_start(dense_sb[:], dense_t[:, bass.ds(c * B, B)]).then_inc(dense_in, 16)
                for n in range(NP):
                    if n == NP // 2 and not first:
                        act.wait_ge(y_out, c * 16)
                    for k in range(EARLY_K, KP):
                        if prep_at(k) == n:
                            high_parts(c, k)
                    for g in range(EARLY_W, NW):
                        if max(0, 2 * g - 6) == n:
                            high_weights(c, g)
                    for blk in range(NZ - 1):
                        if (blk + 1) * ZT // 2 + LAG == n:
                            keep_z(c, blk)
                keep_z(c, NZ - 1)
                if not last:
                    for g in range(EARLY_W):
                        high_weights(c + 1, g)
                act.wait_ge(layers_in, 80)
                for m in range(H1 // P):
                    if not last:
                        high_parts(c + 1, m)
                    act.wait_ge(layer_ps, c * PIECES + (m + 1))
                    nc.scalar.activation(h1[:, m, :], layer_bank(m), ACT.Relu, bias=b1_sb[:, m:m + 1])\
                      .then_inc(layer_sb, 1)
                for m in range(H2 // P):
                    act.wait_ge(layer_ps, c * PIECES + (H1 // P + m + 1))
                    nc.scalar.activation(h2[:, m, :], layer_bank(H1 // P + m), ACT.Relu, bias=b2_sb[:, m:m + 1])\
                      .then_inc(layer_sb, 1)
                act.wait_ge(layer_ps, c * PIECES + PIECES)
                nc.scalar.copy(y_sb[:], layer_bank(PIECES - 1)[0:1, :]).then_inc(layer_sb, 1)
                act.wait_ge(layer_sb, c * PIECES + (FREE_L + PIECES))
                act.dma_start(y[:, bass.ds(c * B, B)], y_sb[:]).then_inc(y_out, 16)

            act.sem_inc(layer_sb, FREE_L)
            for g in range(EARLY_W):
                high_weights(0, g)
            for k in range(EARLY_K):
                high_parts(0, k)
            chunk(0, True, False)
            with act.Fori(1, CHUNKS - 1) as c:
                chunk(c, False, False)
            chunk(CHUNKS - 1, False, True)
            act.wait_ge(y_out, CHUNKS * 16)


        @block.vector
        def _(dve):
            def low_parts(c, k):
                dve.wait_ge(e_hi, c * KP + (k + 1))
                x = x_ps[:, :]
                last = nc.vector.tensor_tensor(p[64:128, 2 * k, :], x[0:64, :], p[0:64, 2 * k, :].bitcast(f32),
                                               ALU.subtract)
                if 2 * k + 1 < FIELDS - 1:
                    last = nc.vector.tensor_tensor(p[0:64, 2 * k + 1, :], x[64:128, :],
                                                   p[64:128, 2 * k + 1, :].bitcast(f32), ALU.subtract)
                last.then_inc(e_ready, 1)

            def low_weights(c, g):
                s = g % W_SLOTS
                dve.wait_ge(hi_ready, c * NW + (g + 1))
                nc.vector.tensor_tensor(w_lo[:, s, :], w_raw[:, s, :], w_hi[:, s, :].bitcast(f32),
                                        ALU.subtract).then_inc(lo_vector, 1)

            def products(c, n):
                k0, k1 = TILES[2 * n][0], TILES[2 * n + 1][0]
                if n >= R_SLOTS:
                    dve.wait_ge(summed, c * NP + (n - R_SLOTS + 1))
                dve.wait_ge(t_ready, c * NP + (n + 1))
                out, t = product[:, n % R_SLOTS, :, :], t_ps[:, n % T_SLOTS, :, :]
                if k0 == k1:
                    both = q[:, k0 % Q_SLOTS:k0 % Q_SLOTS + 1, :].to_broadcast([P, 2, B])
                    nc.vector.tensor_tensor(out, t, both, ALU.mult).then_inc(product_ready, 1)
                else:
                    nc.vector.tensor_tensor(out[:, 0, :], t[:, 0, :], q[:, k0 % Q_SLOTS, :], ALU.mult)
                    nc.vector.tensor_tensor(out[:, 1, :], t[:, 1, :], q[:, k1 % Q_SLOTS, :], ALU.mult)\
                      .then_inc(product_ready, 1)

            dve.sem_inc(lo_vector, FREE_V)
            nc.vector.memset(ones[:], 0.0).then_inc(ones_ready, 1)
            dve.wait_ge(ones_ready, 1)
            nc.vector.memset(ones[0:64, 30:31], 1.0).then_inc(ones_ready, 1)
            nc.vector.memset(ones[64:128, 31:32], 1.0).then_inc(ones_ready, 1)
            def chunk(c, last):
                for n in range(NP):
                    for k in range(EARLY_K, KP):
                        if low_at(k) == n:
                            low_parts(c, k)
                    for g in range(NW):
                        if g % W_SLOTS in W_ON_VECTOR and max(0, 2 * g - 5) == n:
                            low_weights(c, g)
                    products(c, n)
                if not last:
                    for k in range(EARLY_K):
                        low_parts(c + 1, k)

            for k in range(EARLY_K):
                low_parts(0, k)
            with dve.Fori(0, CHUNKS - 1) as c:
                chunk(c, False)
            chunk(CHUNKS - 1, True)

        @block.tensor
        def _(pe):
            def transpose_rows(c, k):
                if k >= 1:
                    pe.wait_ge(e_ready, c * KP + k)
                pe.wait_ge(rows_in[k % G_SLOTS],
                           c * (KP // G_SLOTS * 128) + 128 * (k // G_SLOTS + 1))
                for t in range(ROWT):
                    last = nc.tensor.transpose(x_ps[:, t * P:(t + 1) * P],
                                               rows[:, k % G_SLOTS, t, :], ident[:, 8:8 + P])
                last.then_inc(x_ready, 1)

            def multiply(c, n):
                g = 2 * n // WT
                if 2 * n % WT == 0:
                    done, per_chunk, nth, start = lo_of(g)
                    pe.wait_ge(done, c * per_chunk + (start + nth + 1))
                if n >= T_SLOTS:
                    pe.wait_ge(product_ready, c * NP + (n - T_SLOTS + 1))
                for h in range(2):
                    k, i = TILES[2 * n + h]
                    if i == 0:
                        pe.wait_ge(e_ready, c * KP + (k + 1))
                    w = slice((2 * n + h) % WT * P, ((2 * n + h) % WT + 1) * P)
                    nc.tensor.matmul(t_ps[:, n % T_SLOTS, h, :], w_lo[:, g % W_SLOTS, w], p[:, i, :],
                                     start=True, stop=False)
                    last = nc.tensor.matmul(t_ps[:, n % T_SLOTS, h, :], w_hi[:, g % W_SLOTS, w], p[:, i, :],
                                            start=False, stop=True)
                last.then_inc(t_ready, 1)

            def sum_features(c, n):
                if 2 * n == (NZ - 1) * ZT:
                    pe.wait_ge(dense_in, c * 16 + 16)
                pe.wait_ge(product_ready, c * NP + (n + 1))
                for h in range(2):
                    blk, u = divmod(2 * n + h, ZT)
                    group, s = u % 4, u // 4
                    if u == 0 and blk >= 1:
                        pe.wait_ge(z_ready, c * NZ + blk)
                    last_of_group = min(ZT, NT - blk * ZT) // 4 - 1
                    last = nc.tensor.matmul(z_ps[32 * group:32 * group + 32, :],
                                            ones[:, 30 - 2 * s:62 - 2 * s], product[:, n % R_SLOTS, h, :],
                                            start=(s == 0), stop=(s == last_of_group))
                    if blk == NZ - 1 and u == 0:
                        nc.tensor.matmul(z_ps[0:32, :], ident[0:DENSE, 0:32], dense_sb[:, :],
                                         start=False, stop=False)
                last.then_inc(summed, 1)

            def layer(c, first_piece, pieces, weights, x, kt, early):
                for m in range(pieces):
                    piece = first_piece + m
                    if early:
                        transpose_rows(c + 1, m)
                    for j in range(kt):
                        if first_piece > 0 and m == 0:
                            pe.wait_ge(layer_sb, c * PIECES + (FREE_L + first_piece - kt + j + 1))
                        last = nc.tensor.matmul(layer_bank(piece), weights[:, j, m * P:(m + 1) * P],
                                                x[:, j, :], start=(j == 0), stop=(j == kt - 1))
                    last.then_inc(layer_ps, 1)

            pe.sem_inc(x_ready, FREE_X)
            pe.wait_ge(ident_ready, 2)
            pe.wait_ge(ones_ready, 3)
            def chunk(c, last):
                pe.wait_ge(layer_sb, c * PIECES + FREE_L)
                for n in range(NP):
                    for k in range(EARLY_K, KP):
                        if prep_at(k) == n:
                            transpose_rows(c, k)
                    multiply(c, n)
                    if (n - LAG + 1) % SUMS == 0 and n - LAG + 1 >= SUMS:
                        for s in range(n - LAG + 1 - SUMS, n - LAG + 1):
                            sum_features(c, s)
                for n in range((NP - LAG) // SUMS * SUMS, NP):
                    sum_features(c, n)
                pe.wait_ge(layers_in, 80)
                pe.wait_ge(z_ready, c * NZ + NZ)
                layer(c, 0, H1 // P, w1_sb, z, NZ, not last)
                layer(c, H1 // P, H2 // P, w2_sb, h1, H1 // P, False)
                for j in range(H2 // P):
                    pe.wait_ge(layer_sb, c * PIECES + (FREE_L + PIECES - H2 // P + j))
                    mm = nc.tensor.matmul(layer_bank(PIECES - 1)[0:1, :], w3_sb[:, j:j + 1], h2[:, j, :],
                                          start=(j == 0), stop=(j == H2 // P - 1))
                mm.then_inc(layer_ps, 1)

            for k in range(EARLY_K):
                transpose_rows(0, k)
            with pe.Fori(0, CHUNKS - 1) as c:
                chunk(c, False)
            chunk(CHUNKS - 1, True)


def kernel(**inputs):
    import concourse.bacc as bacc
    from concourse.bass_utils import run_bass_kernel_spmd

    a = {n: np.asarray(v) for n, v in inputs.items()}

    param = a["L0_rec_param"]
    w_tiles = np.zeros((E, NT, 2, E), param.dtype)
    w1 = np.zeros((NZ * P, H1), a["W_top1"].dtype)
    for t, (k, i) in enumerate(TILES):
        for half in range(2):
            if i < 2 * k + half:
                w_tiles[:, t, half] = param[:, pair_index(i, 2 * k + half)].T
                w1[z_row(t, half)] = a["W_top1"][pair_index(i, 2 * k + half)]
    at = (NZ - 1) * P + LAST_ROWS_FREE
    w1[at:at + DENSE] = a["W_top1"][FIELDS * (FIELDS - 1) // 2:]

    def by_partition(x):
        return np.ascontiguousarray(x.reshape(-1, P, x.shape[-1]).transpose(1, 0, 2))

    arrays = {
        "dense_t": np.ascontiguousarray(a["dense_ctx"].T),
        "ids": np.ascontiguousarray(a["ids"]),
        "w_tiles": w_tiles.reshape(E, NT * P),
        "w1": by_partition(w1),
        "b1": np.ascontiguousarray(a["b_top1"].reshape(-1, P).T),
        "w2": by_partition(a["W_top2"]),
        "b2": np.ascontiguousarray(a["b_top2"].reshape(-1, P).T),
        "w3": np.ascontiguousarray(a["W_top3"].reshape(-1, P).T),
    }
    for f in range(FIELDS):
        arrays[f"tbl_{f}"] = np.ascontiguousarray(a[f"tbl_{f}"])

    nc = bacc.Bacc("TRN2", target_bir_lowering=False, num_devices=1)
    d = {n: nc.dram_tensor(n, v.shape, mybir.dt.from_np(v.dtype), kind="ExternalInput").ap()
         for n, v in arrays.items()}
    y = nc.dram_tensor("y", (1, BATCH), mybir.dt.float32, kind="ExternalOutput").ap()
    build(nc, d["dense_t"], d["ids"], [d[f"tbl_{f}"] for f in range(FIELDS)], d["w_tiles"],
          d["w1"], d["b1"], d["w2"], d["b2"], d["w3"], y)
    r = run_bass_kernel_spmd(nc, [arrays], core_ids=[0])
    return r.results[0]["y"].reshape(BATCH, 1)
```

```python
import numpy as np

import concourse.bass as bass
import concourse.mybir as mybir

FIELDS, E, BATCH, DENSE = 40, 64, 2048, 16
H1, H2 = 512, 256
P = 128
B = 512
CHUNKS = BATCH // B
ROWT = B // P
KP = FIELDS // 2
TILES = [(k, i) for k in range(KP) for i in range(2 * k + 1)]
NT = len(TILES)
NP = NT // 2
WT = 4
NW = NT // WT
ZT = 64
NZ = -(-NT // ZT)
LAST_ROWS_FREE = 8

G_SLOTS, Q_SLOTS, W_SLOTS, T_SLOTS, R_SLOTS = 10, 4, 5, 3, 6
SUMS = 2
LAG = 2


def pair_index(i, j):
    return i * FIELDS - i * (i + 1) // 2 + j - i - 1


def z_row(t, half):
    block, u = divmod(t, ZT)
    return block * P + 32 * (u % 4) + 2 * (u // 4) + half


EARLY_K = 4
EARLY_W = 4


def low_on_vector(g, first):
    if not first:
        return g % W_SLOTS == 3
    return g < 24 or g % W_SLOTS in (1, 3) or g < 60 and g % W_SLOTS == 0


def prep_at(k, first):
    if first and k < 8:
        return max(0, k * k // 2 - (k > 3))
    return (k * k - 12) // 2 if k >= EARLY_K else None


def low_at(k, first):
    return min(prep_at(k, first) + 2, k * k // 2) if first or k >= EARLY_K else None


def build(nc, dense_t, ids, tables, w_tiles, w1, b1, w2, b2, w3, y):
    from contextlib import ExitStack

    f32, f32r, i32 = mybir.dt.float32, mybir.dt.float32r, mybir.dt.int32
    ALU, ACT = mybir.AluOpType, mybir.ActivationFunctionType

    with ExitStack() as ctx:
        def sb(name, shape, dt=f32):
            return ctx.enter_context(nc.sbuf_tensor(name, shape, dt))

        def sem(name):
            return ctx.enter_context(nc.semaphore(name))

        ids_all = sb("ids_all", [P, BATCH // P, FIELDS], i32)
        ids_early = sb("ids_early", [P, ROWT, FIELDS // 2], i32)
        ids_late = sb("ids_late", [P, ROWT, FIELDS // 2], i32)
        rows = sb("rows", [P, G_SLOTS, ROWT, 2 * E])
        ident = sb("ident", [P, 8 + P])
        ones = sb("ones", [P, 62])
        q = sb("q", [P, Q_SLOTS, B])
        p = sb("p", [P, FIELDS - 1, B], f32r)
        w_raw = sb("w_raw", [P, W_SLOTS, WT * P])
        w_hi = sb("w_hi", [P, W_SLOTS, WT * P], f32r)
        w_lo = sb("w_lo", [P, W_SLOTS, WT * P], f32r)
        product = sb("product", [P, R_SLOTS, 2, B])
        z = sb("z", [P, NZ, B])
        h1 = product[:, 0:H1 // P // 2, :, :].rearrange("p s h b -> p (s h) b")
        dense_sb = sb("dense_sb", [DENSE, B])
        w1_sb = sb("w1_sb", [P, NZ, H1])
        w2_sb = sb("w2_sb", [P, H1 // P, H2])
        w3_sb = sb("w3_sb", [P, H2 // P])
        b1_sb = sb("b1_sb", [P, H1 // P])
        b2_sb = sb("b2_sb", [P, H2 // P])
        h2 = z[:, 0:H2 // P, :]
        y_sb = sb("y_sb", [1, B])
        t_ps = ctx.enter_context(nc.psum_tensor("t_ps", [P, T_SLOTS, 2, B], f32))
        z_ps = ctx.enter_context(nc.psum_tensor("z_ps", [P, B], f32))
        x_ps = ctx.enter_context(nc.psum_tensor("x_ps", [P, B], f32))

        ids_in = sem("ids_in")
        early_ids_in = sem("early_ids_in")
        late_ids_in = sem("late_ids_in")
        layers_in = sem("layers_in")
        dense_in = sem("dense_in")
        y_out = sem("y_out")
        ident_ready = sem("ident_ready")
        ones_ready = sem("ones_ready")
        ids_ready = sem("ids_ready")
        lookups_begun = sem("lookups_begun")
        raw_in = [sem(f"raw_in{s}") for s in range(W_SLOTS)]
        w_ready = [sem(f"w_ready{s}") for s in range(W_SLOTS)]
        rows_in = [sem(f"rows_in{s}") for s in range(G_SLOTS)]
        x_ready = sem("x_ready")
        FREE_X, FREE_L = G_SLOTS, 2
        e_hi = sem("e_hi")
        e_ready = sem("e_ready")
        hi_ready = sem("hi_ready")
        t_ready = sem("t_ready")
        product_ready = sem("product_ready")
        summed = sem("summed")
        z_ready = sem("z_ready")
        layer_ps = sem("layer_ps")
        layer_sb = sem("layer_sb")
        PIECES = H1 // P + H2 // P + 1

        block = ctx.enter_context(nc.Block())

        def layer_bank(piece):
            return t_ps[:, piece // 2 % T_SLOTS, piece % 2, :]

        KW = NW // W_SLOTS

        @block.sync
        def _(sp):
            by_row = ids.rearrange("(t p) f -> p t f", p=P)
            sp.dma_start(ids_early[:], by_row[:, 0:ROWT, 0:FIELDS // 2]).then_inc(early_ids_in, 16)

            def load_granules(c, j, first=False):
                for s in range(W_SLOTS):
                    if not first:
                        sp.wait_ge(w_ready[s], c * KW + j)
                    col = j * (W_SLOTS * WT * P) + s * WT * P
                    for half in range(2):
                        sp.dma_start(w_raw[64 * half:64 * half + 64, s, :], w_tiles[:, bass.ds(col, WT * P)])\
                          .then_inc(raw_in[s], 16)

            load_granules(0, 0, True)
            sp.dma_start(ids_late[:], by_row[:, 0:ROWT, FIELDS // 2:FIELDS]).then_inc(late_ids_in, 16)
            with sp.Fori(1, KW // 2) as j:
                load_granules(0, j)
            sp.dma_start(ids_all[:], by_row).then_inc(ids_in, 16)
            sp.dma_start(w1_sb[:], w1).then_inc(layers_in, 16)
            sp.dma_start(b1_sb[:], b1).then_inc(layers_in, 16)
            sp.dma_start(w2_sb[:], w2).then_inc(layers_in, 16)
            sp.dma_start(b2_sb[:], b2).then_inc(layers_in, 16)
            sp.dma_start(w3_sb[:], w3).then_inc(layers_in, 16)
            with sp.Fori(KW // 2, KW) as j:
                load_granules(0, j)
            with sp.Fori(1, CHUNKS) as c:
                with sp.Fori(0, KW) as j:
                    load_granules(c, j)

        @block.gpsimd
        def _(pool):
            def copy_ids(c, late, nth):
                dst = ids_late if late else ids_early
                src = ids_all[:, bass.ds(c * ROWT, ROWT), (FIELDS // 2) * late:(FIELDS // 2) * (late + 1)]
                nc.gpsimd.tensor_copy(dst[:], src).then_inc(ids_ready, 1)
                pool.wait_ge(ids_ready, nth)
                pool.sem_inc(lookups_begun, 1)

            def lookup(c, k, m):
                t, h = divmod(m, 2)
                if m == 0:
                    pool.wait_ge(x_ready, c * KP + (k + 1))
                    pool.sem_inc(lookups_begun, 1)
                late, col = divmod(2 * k + h, FIELDS // 2)
                idx = (ids_late if late else ids_early)[:, t, col:col + 1]
                nc.gpsimd.indirect_dma_start(
                    rows[:, k % G_SLOTS, t, h * E:(h + 1) * E], None, tables[2 * k + h],
                    bass.IndirectOffsetOnAxis(idx, axis=0)).then_inc(rows_in[k % G_SLOTS], 16)

            def low_weights(c, g):
                s = g % W_SLOTS
                pool.wait_ge(hi_ready, c * NW + (g + 1))
                nc.gpsimd.tensor_tensor(w_lo[:, s, :], w_raw[:, s, :], w_hi[:, s, :].bitcast(f32),
                                        ALU.subtract).then_inc(w_ready[s], 1)

            def lookup_at(k, m, first):
                if first:
                    return 0 if k < 4 else max(0, k * k // 2 - 14) if k < 8 else 6 * k - 31 + m * 3 // 4
                return (k - KP // 2) * 10 + m if k >= KP // 2 else -1

            def chunk(c, first, last):
                for n in range(NP):
                    if first and n == lookup_at(KP // 2, 0, True):
                        pool.wait_ge(late_ids_in, 16)
                        pool.sem_inc(lookups_begun, 1)
                    if n == 0 and not first:
                        copy_ids(c, 1, c * 2)
                    if n == NP // 2 and not last:
                        if first:
                            pool.wait_ge(ids_in, 16)
                        copy_ids(c + 1, 0, c * 2 + 1)
                    for k in range(KP):
                        for m in range(2 * ROWT):
                            if lookup_at(k, m, first) == n:
                                lookup(c, k, m)
                            if k < KP // 2 and not last and NP // 2 + (8 if first else 10) * k + m == n:
                                lookup(c + 1, k, m)
                    for g in range(NW):
                        if not low_on_vector(g, first) and max(0, 2 * g - 5) == n:
                            low_weights(c, g)

            nc.gpsimd.memset(ident[:], 0.0).then_inc(ident_ready, 1)
            pool.wait_ge(ident_ready, 1)
            nc.gpsimd.affine_select(out=ident[:], in_=ident[:], compare_op=ALU.not_equal, fill=1.0, base=8,
                                    pattern=[[-1, 8 + P]], channel_multiplier=1).then_inc(ident_ready, 1)
            pool.wait_ge(ident_ready, 2)
            pool.wait_ge(early_ids_in, 16)
            pool.sem_inc(lookups_begun, 1)
            chunk(0, True, False)
            with pool.Fori(1, CHUNKS - 1) as c:
                chunk(c, False, False)
            chunk(CHUNKS - 1, False, True)

        @block.scalar
        def _(act):
            def high_parts(c, k):
                act.wait_ge(x_ready, c * KP + (FREE_X + k + 1))
                if k >= Q_SLOTS:
                    act.wait_ge(product_ready, c * NP + (k - Q_SLOTS + 1) ** 2 // 2 + 1)
                x = x_ps[:, :]
                nc.scalar.copy(p[0:64, 2 * k, :], x[0:64, :])
                if 2 * k + 1 < FIELDS - 1:
                    nc.scalar.copy(p[64:128, 2 * k + 1, :], x[64:128, :])
                nc.scalar.copy(q[:, k % Q_SLOTS, :], x).then_inc(e_hi, 1)

            def high_weights(c, g):
                s = g % W_SLOTS
                if g >= W_SLOTS:
                    act.wait_ge(t_ready, c * NP + 2 * (g - W_SLOTS) + 2)
                act.wait_ge(raw_in[s], c * (32 * KW) + 32 * (g // W_SLOTS + 1))
                nc.scalar.copy(w_hi[:, s, :], w_raw[:, s, :]).then_inc(hi_ready, 1)

            def keep_z(c, block_):
                act.wait_ge(summed, c * NP + min((block_ + 1) * ZT // 2, NP))
                nc.scalar.copy(z[:, block_, :], z_ps[:, :]).then_inc(z_ready, 1)

            def chunk(c, first, last):
                act.dma_start(dense_sb[:], dense_t[:, bass.ds(c * B, B)]).then_inc(dense_in, 16)
                for n in range(NP):
                    if n == NP // 2 and not first:
                        act.wait_ge(y_out, c * 16)
                    for blk in range(NZ - 1):
                        if (blk + 1) * ZT // 2 + LAG == n:
                            keep_z(c, blk)
                    for k in range(KP):
                        if prep_at(k, first) == n:
                            high_parts(c, k)
                    for g in range(EARLY_W, NW):
                        if max(0, 2 * g - 6) == n:
                            high_weights(c, g)
                keep_z(c, NZ - 1)
                if not last:
                    for g in range(EARLY_W):
                        high_weights(c + 1, g)
                act.wait_ge(layers_in, 80)
                for m in range(H1 // P):
                    if not last:
                        high_parts(c + 1, m)
                    act.wait_ge(layer_ps, c * PIECES + (m + 1))
                    nc.scalar.activation(h1[:, m, :], layer_bank(m), ACT.Relu, bias=b1_sb[:, m:m + 1])\
                      .then_inc(layer_sb, 1)
                for m in range(H2 // P):
                    act.wait_ge(layer_ps, c * PIECES + (H1 // P + m + 1))
                    nc.scalar.activation(h2[:, m, :], layer_bank(H1 // P + m), ACT.Relu, bias=b2_sb[:, m:m + 1])\
                      .then_inc(layer_sb, 1)
                act.wait_ge(layer_ps, c * PIECES + PIECES)
                nc.scalar.copy(y_sb[:], layer_bank(PIECES - 1)[0:1, :]).then_inc(layer_sb, 1)
                act.wait_ge(layer_sb, c * PIECES + (FREE_L + PIECES))
                act.dma_start(y[:, bass.ds(c * B, B)], y_sb[:]).then_inc(y_out, 16)

            act.sem_inc(layer_sb, FREE_L)
            for g in range(EARLY_W):
                high_weights(0, g)
            chunk(0, True, False)
            with act.Fori(1, CHUNKS - 1) as c:
                chunk(c, False, False)
            chunk(CHUNKS - 1, False, True)
            act.wait_ge(y_out, CHUNKS * 16)

        @block.vector
        def _(dve):
            def low_parts(c, k):
                dve.wait_ge(e_hi, c * KP + (k + 1))
                x = x_ps[:, :]
                last = nc.vector.tensor_tensor(p[64:128, 2 * k, :], x[0:64, :], p[0:64, 2 * k, :].bitcast(f32),
                                               ALU.subtract)
                if 2 * k + 1 < FIELDS - 1:
                    last = nc.vector.tensor_tensor(p[0:64, 2 * k + 1, :], x[64:128, :],
                                                   p[64:128, 2 * k + 1, :].bitcast(f32), ALU.subtract)
                last.then_inc(e_ready, 1)

            def low_weights(c, g):
                s = g % W_SLOTS
                dve.wait_ge(hi_ready, c * NW + (g + 1))
                nc.vector.tensor_tensor(w_lo[:, s, :], w_raw[:, s, :], w_hi[:, s, :].bitcast(f32),
                                        ALU.subtract).then_inc(w_ready[s], 1)

            def products(c, n):
                k0, k1 = TILES[2 * n][0], TILES[2 * n + 1][0]
                if n >= R_SLOTS:
                    dve.wait_ge(summed, c * NP + (n - R_SLOTS + 1))
                dve.wait_ge(t_ready, c * NP + (n + 1))
                out, t = product[:, n % R_SLOTS, :, :], t_ps[:, n % T_SLOTS, :, :]
                if k0 == k1:
                    both = q[:, k0 % Q_SLOTS:k0 % Q_SLOTS + 1, :].to_broadcast([P, 2, B])
                    nc.vector.tensor_tensor(out, t, both, ALU.mult).then_inc(product_ready, 1)
                else:
                    nc.vector.tensor_tensor(out[:, 0, :], t[:, 0, :], q[:, k0 % Q_SLOTS, :], ALU.mult)
                    nc.vector.tensor_tensor(out[:, 1, :], t[:, 1, :], q[:, k1 % Q_SLOTS, :], ALU.mult)\
                      .then_inc(product_ready, 1)

            nc.vector.memset(ones[:], 0.0).then_inc(ones_ready, 1)
            dve.wait_ge(ones_ready, 1)
            nc.vector.memset(ones[0:64, 30:31], 1.0).then_inc(ones_ready, 1)
            nc.vector.memset(ones[64:128, 31:32], 1.0).then_inc(ones_ready, 1)

            def chunk(c, first, last):
                for n in range(NP):
                    for k in range(KP):
                        if low_at(k, first) == n:
                            low_parts(c, k)
                    for g in range(NW):
                        if low_on_vector(g, first) and max(0, 2 * g - 5) == n:
                            low_weights(c, g)
                    products(c, n)
                if not last:
                    for k in range(EARLY_K):
                        low_parts(c + 1, k)

            chunk(0, True, False)
            with dve.Fori(1, CHUNKS - 1) as c:
                chunk(c, False, False)
            chunk(CHUNKS - 1, False, True)

        @block.tensor
        def _(pe):
            def transpose_rows(c, k):
                if k >= 1:
                    pe.wait_ge(e_ready, c * KP + k)
                pe.wait_ge(rows_in[k % G_SLOTS],
                           c * (KP // G_SLOTS * 128) + 128 * (k // G_SLOTS + 1))
                for t in range(ROWT):
                    last = nc.tensor.transpose(x_ps[:, t * P:(t + 1) * P],
                                               rows[:, k % G_SLOTS, t, :], ident[:, 8:8 + P])
                last.then_inc(x_ready, 1)

            def multiply(c, n):
                g = 2 * n // WT
                if 2 * n % WT == 0:
                    pe.wait_ge(w_ready[g % W_SLOTS], c * KW + (g // W_SLOTS + 1))
                if n >= T_SLOTS:
                    pe.wait_ge(product_ready, c * NP + (n - T_SLOTS + 1))
                for h in range(2):
                    k, i = TILES[2 * n + h]
                    if i == 0:
                        pe.wait_ge(e_ready, c * KP + (k + 1))
                    w = slice((2 * n + h) % WT * P, ((2 * n + h) % WT + 1) * P)
                    nc.tensor.matmul(t_ps[:, n % T_SLOTS, h, :], w_lo[:, g % W_SLOTS, w], p[:, i, :],
                                     start=True, stop=False)
                    last = nc.tensor.matmul(t_ps[:, n % T_SLOTS, h, :], w_hi[:, g % W_SLOTS, w], p[:, i, :],
                                            start=False, stop=True)
                last.then_inc(t_ready, 1)

            def sum_features(c, n):
                if 2 * n == (NZ - 1) * ZT:
                    pe.wait_ge(dense_in, c * 16 + 16)
                pe.wait_ge(product_ready, c * NP + (n + 1))
                for h in range(2):
                    blk, u = divmod(2 * n + h, ZT)
                    group, s = u % 4, u // 4
                    if u == 0 and blk >= 1:
                        pe.wait_ge(z_ready, c * NZ + blk)
                    last_of_group = min(ZT, NT - blk * ZT) // 4 - 1
                    last = nc.tensor.matmul(z_ps[32 * group:32 * group + 32, :],
                                            ones[:, 30 - 2 * s:62 - 2 * s], product[:, n % R_SLOTS, h, :],
                                            start=(s == 0), stop=(s == last_of_group))
                    if blk == NZ - 1 and u == 0:
                        nc.tensor.matmul(z_ps[0:32, :], ident[0:DENSE, 0:32], dense_sb[:, :],
                                         start=False, stop=False)
                last.then_inc(summed, 1)

            def layer(c, first_piece, pieces, weights, x, kt, early):
                for m in range(pieces):
                    piece = first_piece + m
                    if early:
                        transpose_rows(c + 1, m)
                    for j in range(kt):
                        if first_piece > 0 and m == 0:
                            pe.wait_ge(layer_sb, c * PIECES + (FREE_L + first_piece - kt + j + 1))
                        last = nc.tensor.matmul(layer_bank(piece), weights[:, j, m * P:(m + 1) * P],
                                                x[:, j, :], start=(j == 0), stop=(j == kt - 1))
                    last.then_inc(layer_ps, 1)

            pe.sem_inc(x_ready, FREE_X)
            pe.wait_ge(ident_ready, 2)
            pe.wait_ge(ones_ready, 3)

            def chunk(c, first, last):
                pe.wait_ge(layer_sb, c * PIECES + FREE_L)
                for n in range(NP):
                    for k in range(KP):
                        if prep_at(k, first) == n:
                            transpose_rows(c, k)
                    multiply(c, n)
                    if (n - LAG + 1) % SUMS == 0 and n - LAG + 1 >= SUMS:
                        for s in range(n - LAG + 1 - SUMS, n - LAG + 1):
                            sum_features(c, s)
                for n in range((NP - LAG) // SUMS * SUMS, NP):
                    sum_features(c, n)
                pe.wait_ge(layers_in, 80)
                pe.wait_ge(z_ready, c * NZ + NZ)
                layer(c, 0, H1 // P, w1_sb, z, NZ, not last)
                layer(c, H1 // P, H2 // P, w2_sb, h1, H1 // P, False)
                for j in range(H2 // P):
                    pe.wait_ge(layer_sb, c * PIECES + (FREE_L + PIECES - H2 // P + j))
                    mm = nc.tensor.matmul(layer_bank(PIECES - 1)[0:1, :], w3_sb[:, j:j + 1], h2[:, j, :],
                                          start=(j == 0), stop=(j == H2 // P - 1))
                mm.then_inc(layer_ps, 1)

            chunk(0, True, False)
            with pe.Fori(1, CHUNKS - 1) as c:
                chunk(c, False, False)
            chunk(CHUNKS - 1, False, True)


def kernel(**inputs):
    import concourse.bacc as bacc
    from concourse.bass_utils import run_bass_kernel_spmd

    a = {n: np.asarray(v) for n, v in inputs.items()}

    param = a["L0_rec_param"]
    w_tiles = np.zeros((E, NT, 2, E), param.dtype)
    w1 = np.zeros((NZ * P, H1), a["W_top1"].dtype)
    for t, (k, i) in enumerate(TILES):
        for half in range(2):
            if i < 2 * k + half:
                w_tiles[:, t, half] = param[:, pair_index(i, 2 * k + half)].T
                w1[z_row(t, half)] = a["W_top1"][pair_index(i, 2 * k + half)]
    at = (NZ - 1) * P + LAST_ROWS_FREE
    w1[at:at + DENSE] = a["W_top1"][FIELDS * (FIELDS - 1) // 2:]

    def by_partition(x):
        return np.ascontiguousarray(x.reshape(-1, P, x.shape[-1]).transpose(1, 0, 2))

    arrays = {
        "dense_t": np.ascontiguousarray(a["dense_ctx"].T),
        "ids": np.ascontiguousarray(a["ids"]),
        "w_tiles": w_tiles.reshape(E, NT * P),
        "w1": by_partition(w1),
        "b1": np.ascontiguousarray(a["b_top1"].reshape(-1, P).T),
        "w2": by_partition(a["W_top2"]),
        "b2": np.ascontiguousarray(a["b_top2"].reshape(-1, P).T),
        "w3": np.ascontiguousarray(a["W_top3"].reshape(-1, P).T),
    }
    for f in range(FIELDS):
        arrays[f"tbl_{f}"] = np.ascontiguousarray(a[f"tbl_{f}"])

    nc = bacc.Bacc("TRN2", target_bir_lowering=False, num_devices=1)
    d = {n: nc.dram_tensor(n, v.shape, mybir.dt.from_np(v.dtype), kind="ExternalInput").ap()
         for n, v in arrays.items()}
    y = nc.dram_tensor("y", (1, BATCH), mybir.dt.float32, kind="ExternalOutput").ap()
    build(nc, d["dense_t"], d["ids"], [d[f"tbl_{f}"] for f in range(FIELDS)], d["w_tiles"],
          d["w1"], d["b1"], d["w2"], d["b2"], d["w3"], y)
    r = run_bass_kernel_spmd(nc, [arrays], core_ids=[0])
    return r.results[0]["y"].reshape(BATCH, 1)
```
